# Optimizing a Trainium2 kernel written in Bass

```python
import numpy as np
import jax
import jax.numpy as jnp

def _softmax(x, axis=-1):
    return jax.nn.softmax(x, axis=axis)

def _gelu(x):
    return jax.nn.gelu(x, approximate=True)

def _silu(x):
    return jax.nn.silu(x)

def _sigmoid(x):
    return jax.nn.sigmoid(x)

def _layernorm(x, axis=-1, eps=1e-05):
    m = jnp.mean(x, axis=axis, keepdims=True)
    v = jnp.var(x, axis=axis, keepdims=True)
    return (x - m) / jnp.sqrt(v + eps)

def _scatter_add(tgt, idx, src, axis=0):
    return tgt.at[idx].add(src)

def _segment_sum(src, seg, n):
    return jax.ops.segment_sum(src, seg, n)
kernel_name = 'mk_rec_standalone_d1_rec_r8_0dc4d7'

def setup_inputs(seed: int=0):
    np.random.seed(seed)
    _w = jnp.asarray

    def _rec_inputs():
        import jax
        import jax.numpy as jnp
        _rk = jax.random.key(seed)
        r_x_idx = jnp.stack([jax.random.randint(jax.random.fold_in(jax.random.fold_in(_rk, 1), 0), (2048,), 86, 99990, jnp.int32), jax.random.randint(jax.random.fold_in(jax.random.fold_in(_rk, 1), 1), (2048,), 10, 99946, jnp.int32), jax.random.randint(jax.random.fold_in(jax.random.fold_in(_rk, 1), 2), (2048,), 78, 99986, jnp.int32), jax.random.randint(jax.random.fold_in(jax.random.fold_in(_rk, 1), 3), (2048,), 62, 99977, jnp.int32), jax.random.randint(jax.random.fold_in(jax.random.fold_in(_rk, 1), 4), (2048,), 1, 99988, jnp.int32), jax.random.randint(jax.random.fold_in(jax.random.fold_in(_rk, 1), 5), (2048,), 1, 99988, jnp.int32), jax.random.randint(jax.random.fold_in(jax.random.fold_in(_rk, 1), 6), (2048,), 18, 99973, jnp.int32), jax.random.randint(jax.random.fold_in(jax.random.fold_in(_rk, 1), 7), (2048,), 17, 99988, jnp.int32), jax.random.randint(jax.random.fold_in(jax.random.fold_in(_rk, 1), 8), (2048,), 44, 99975, jnp.int32), jax.random.randint(jax.random.fold_in(jax.random.fold_in(_rk, 1), 9), (2048,), 28, 99998, jnp.int32), jax.random.randint(jax.random.fold_in(jax.random.fold_in(_rk, 1), 10), (2048,), 5, 99993, jnp.int32), jax.random.randint(jax.random.fold_in(jax.random.fold_in(_rk, 1), 11), (2048,), 32, 99985, jnp.int32), jax.random.randint(jax.random.fold_in(jax.random.fold_in(_rk, 1), 12), (2048,), 51, 99951, jnp.int32), jax.random.randint(jax.random.fold_in(jax.random.fold_in(_rk, 1), 13), (2048,), 129, 99982, jnp.int32), jax.random.randint(jax.random.fold_in(jax.random.fold_in(_rk, 1), 14), (2048,), 3, 99966, jnp.int32), jax.random.randint(jax.random.fold_in(jax.random.fold_in(_rk, 1), 15), (2048,), 15, 99987, jnp.int32), jax.random.randint(jax.random.fold_in(jax.random.fold_in(_rk, 1), 16), (2048,), 22, 99998, jnp.int32), jax.random.randint(jax.random.fold_in(jax.random.fold_in(_rk, 1), 17), (2048,), 31, 99949, jnp.int32), jax.random.randint(jax.random.fold_in(jax.random.fold_in(_rk, 1), 18), (2048,), 15, 99996, jnp.int32), jax.random.randint(jax.random.fold_in(jax.random.fold_in(_rk, 1), 19), (2048,), 6, 99942, jnp.int32), jax.random.randint(jax.random.fold_in(jax.random.fold_in(_rk, 1), 20), (2048,), 28, 99986, jnp.int32), jax.random.randint(jax.random.fold_in(jax.random.fold_in(_rk, 1), 21), (2048,), 10, 99991, jnp.int32), jax.random.randint(jax.random.fold_in(jax.random.fold_in(_rk, 1), 22), (2048,), 7, 99965, jnp.int32), jax.random.randint(jax.random.fold_in(jax.random.fold_in(_rk, 1), 23), (2048,), 15, 99963, jnp.int32), jax.random.randint(jax.random.fold_in(jax.random.fold_in(_rk, 1), 24), (2048,), 29, 99990, jnp.int32), jax.random.randint(jax.random.fold_in(jax.random.fold_in(_rk, 1), 25), (2048,), 42, 99986, jnp.int32)], axis=1)
        return r_x_idx
    r_x_idx = _rec_inputs()

    def _L0_rec_setup():
        import jax, jax.numpy as jnp
        import numpy as np
        N = 512
        F = 26
        V = 12500
        D = 16
        H = 400
        K = 128
        key = jax.random.key(seed)
        ks = jax.random.split(key, 16)
        s = 0.05
        return {'x_idx': jax.random.randint(ks[0], (N, F), 0, V, dtype=jnp.int32), 'embed_table': jax.random.normal(ks[1], (F, V, D), dtype=jnp.float32) * 0.01, 'w1_table': jax.random.normal(ks[2], (F, V), dtype=jnp.float32) * 0.01, 'w1_bias': jnp.zeros((1,), dtype=jnp.float32), 'mlp_w1': jax.random.normal(ks[3], (F * D, H), dtype=jnp.float32) * s, 'mlp_b1': jnp.zeros((H,), dtype=jnp.float32), 'mlp_w2': jax.random.normal(ks[4], (H, H), dtype=jnp.float32) * s, 'mlp_b2': jnp.zeros((H,), dtype=jnp.float32), 'mlp_w3': jax.random.normal(ks[5], (H, 1), dtype=jnp.float32) * s, 'mlp_b3': jnp.zeros((1,), dtype=jnp.float32), 'cin_w0': jax.random.normal(ks[6], (K, F, F), dtype=jnp.float32) * s, 'cin_w1': jax.random.normal(ks[7], (K, K, F), dtype=jnp.float32) * s, 'cin_w2': jax.random.normal(ks[8], (K, K, F), dtype=jnp.float32) * s, 'lin_w': jax.random.normal(ks[9], (3 * K, 1), dtype=jnp.float32) * s, 'lin_b': jnp.zeros((1,), dtype=jnp.float32)}
    _L0_rec_all = _L0_rec_setup()
    _L0_rec_in = {k: v for k, v in _L0_rec_all.items() if k in ('embed_table', 'w1_table', 'w1_bias', 'mlp_w1', 'mlp_b1', 'mlp_w2', 'mlp_b2', 'mlp_w3', 'mlp_b3', 'cin_w0', 'cin_w1', 'cin_w2', 'lin_w', 'lin_b')}
    del _L0_rec_all
    return {'r_x_idx': r_x_idx, 'L0_rec_embed_table': _L0_rec_in['embed_table'], 'L0_rec_w1_table': _L0_rec_in['w1_table'], 'L0_rec_w1_bias': _L0_rec_in['w1_bias'], 'L0_rec_mlp_w1': _L0_rec_in['mlp_w1'], 'L0_rec_mlp_b1': _L0_rec_in['mlp_b1'], 'L0_rec_mlp_w2': _L0_rec_in['mlp_w2'], 'L0_rec_mlp_b2': _L0_rec_in['mlp_b2'], 'L0_rec_mlp_w3': _L0_rec_in['mlp_w3'], 'L0_rec_mlp_b3': _L0_rec_in['mlp_b3'], 'L0_rec_cin_w0': _L0_rec_in['cin_w0'], 'L0_rec_cin_w1': _L0_rec_in['cin_w1'], 'L0_rec_cin_w2': _L0_rec_in['cin_w2'], 'L0_rec_lin_w': _L0_rec_in['lin_w'], 'L0_rec_lin_b': _L0_rec_in['lin_b']}

def reference(r_x_idx, L0_rec_embed_table, L0_rec_w1_table, L0_rec_w1_bias, L0_rec_mlp_w1, L0_rec_mlp_b1, L0_rec_mlp_w2, L0_rec_mlp_b2, L0_rec_mlp_w3, L0_rec_mlp_b3, L0_rec_cin_w0, L0_rec_cin_w1, L0_rec_cin_w2, L0_rec_lin_w, L0_rec_lin_b):
    import jax
    import jax.numpy as jnp

    def _L0_rec_ref(x_idx, embed_table, w1_table, w1_bias, mlp_w1, mlp_b1, mlp_w2, mlp_b2, mlp_w3, mlp_b3, cin_w0, cin_w1, cin_w2, lin_w, lin_b):
        import jax, jax.numpy as jnp
        import numpy as np
        N = 512
        F = 26
        V = 12500
        D = 16
        H = 400
        K = 128
        n = x_idx.shape[0]
        f_ix = jnp.arange(F)
        emb = embed_table[f_ix, x_idx]
        lin1 = w1_table[f_ix, x_idx].sum(axis=1, keepdims=True) + w1_bias
        s = emb.sum(axis=1)
        fm = 0.5 * ((s * s).sum(-1) - (emb * emb).sum(axis=(1, 2)))[:, None]
        h = emb.reshape(n, F * D)
        h = jax.nn.relu(h @ mlp_w1 + mlp_b1)
        h = jax.nn.relu(h @ mlp_w2 + mlp_b2)
        mlp_out = h @ mlp_w3 + mlp_b3
        deepfm_result = lin1 + fm + mlp_out
        x0 = emb.transpose(0, 2, 1)
        last = x0
        feats = []
        for W in (cin_w0, cin_w1, cin_w2):
            last = jnp.einsum('ndl,ndf,klf->ndk', last, x0, W)
            feats.append(last)
        cin_out = jnp.concatenate(feats, axis=-1).sum(axis=1)
        cin_result = cin_out @ lin_w + lin_b
        return deepfm_result + cin_result
    y = _L0_rec_ref(r_x_idx, L0_rec_embed_table, L0_rec_w1_table, L0_rec_w1_bias, L0_rec_mlp_w1, L0_rec_mlp_b1, L0_rec_mlp_w2, L0_rec_mlp_b2, L0_rec_mlp_w3, L0_rec_mlp_b3, L0_rec_cin_w0, L0_rec_cin_w1, L0_rec_cin_w2, L0_rec_lin_w, L0_rec_lin_b)
    return y

_drawn_inputs = setup_inputs


def setup_inputs(seed=0):
    import zlib

    import numpy as np

    out = dict(_drawn_inputs(seed))
    spreads = {'L0_rec_mlp_b1': (0.0, 0.1), 'L0_rec_mlp_b2': (0.0, 0.1)}
    factors = {'L0_rec_cin_w0': 8.0, 'L0_rec_cin_w1': 8.0, 'L0_rec_cin_w2': 64.0, 'L0_rec_lin_w': 5.769}
    for name, (base, spread) in spreads.items():
        noise = np.random.default_rng([zlib.crc32(name.encode()), seed]).standard_normal(out[name].shape)
        drawn = base * np.exp(spread * noise) if base else spread * noise
        out[name] = jnp.asarray(drawn.astype(out[name].dtype))
    for name, factor in factors.items():
        out[name] = (out[name] * factor).astype(out[name].dtype)
    return out
```

```python
from contextlib import ExitStack

import concourse.bass as bass
from concourse import mybir

F32 = mybir.dt.float32
F32R = mybir.dt.float32r
I32 = mybir.dt.int32
ALU = mybir.AluOpType
ACT = mybir.ActivationFunctionType
AX = mybir.AxisListType

P = 128
BANK = 512
QUAD = BANK // P


def deepfm_cin_kernel(nc, x_idx, rows, w1_bias, mlp_w1, mlp_b1, mlp_w2, mlp_b2, mlp_w3, mlp_b3,
                      cin_w0, cin_w1, cin_w2, lin_w, lin_b, out):
    N, F = x_idx.shape
    R = rows.shape[1]
    D = R - 1
    V = rows.shape[0] // F
    K = cin_w0.shape[0]
    H = mlp_w1.shape[1]
    T = N // P
    BUF = 2
    NQ = D // QUAD
    HALF = F // 2
    NPAIR = F * (F + 1) // 2
    ZW = NPAIR + F + 1
    NC = 3
    ZC = ZW // NC
    NU = NQ * NC
    EC = F * D // 4
    HC = H // 4
    LAST, Q = 0, 1
    assert K == P and ZC * NC == ZW and ZC <= P and N % (P * BUF) == 0

    with ExitStack() as ctx:
        def sb(name, shape, dt=F32):
            return ctx.enter_context(nc.sbuf_tensor(name, shape, dt))

        def psum(name):
            return ctx.enter_context(nc.psum_tensor(name, [P, BANK], F32))

        def sem(name):
            return ctx.enter_context(nc.semaphore(name))

        idx_raw = sb("idx_raw", [P, T, F], I32)
        idx_wrap = sb("idx_wrap", [P, T, F])
        idx_sum = sb("idx_sum", [P, T, F])
        row_base = sb("row_base", [P, F], I32)
        row_ix = sb("row_ix", [P, T + BUF, F], I32)
        ix_now = [sb(f"ix_now{b}", [P, F], I32) for b in range(BUF)]
        emb = [sb(f"emb{b}", [P, F + HALF, R]) for b in range(BUF)]
        z = sb("z", [P, D, ZW])
        z_hi = sb("z_hi", [P, 2, BANK], F32R)
        z_lo = sb("z_lo", [P, 2, BANK], F32R)
        last_sb = sb("last_sb", [P, 2, BANK])
        prod = sb("prod", [P, 2, BANK])
        w0 = sb("w0", [P, F, F])
        w1 = sb("w1", [P, K, F])
        w2 = sb("w2", [P, K, F])
        lin = sb("lin", [P, 3])
        m_lin2 = sb("m_lin2", [P, F + 1])
        b_a = sb("b_a", [P, F, F + 1])
        sym = [sb("sym_w0", [P, F, 2 * F]), sb("sym_b", [P, F, 2 * F])]
        zw = [sb("zw_last", [P, ZW]), sb("zw_q", [P, ZW])]
        zw_hi = sb("zw_hi", [P, 2, NC, P], F32R)
        zw_lo = sb("zw_lo", [P, 2, NC, P], F32R)
        m1_raw = sb("m1_raw", [P, 4, H])
        m1_hi = sb("m1_hi", [P, 4, H], F32R)
        m1_lo = sb("m1_lo", [P, 4, H], F32R)
        m2_raw = sb("m2_raw", [P, 4, H])
        m2_hi = sb("m2_hi", [P, 4, H], F32R)
        m2_lo = sb("m2_lo", [P, 4, H], F32R)
        w3_all = sb("w3_all", [P, H])
        by_pos = sb("by_pos", [P, D * F])
        embt_hi = sb("embt_hi", [P, 4, P], F32R)
        embt_lo = sb("embt_lo", [P, 4, P], F32R)
        h1 = sb("h1", [P, H])
        h1t_hi = sb("h1t_hi", [P, 4, P], F32R)
        h1t_lo = sb("h1t_lo", [P, 4, P], F32R)
        h2w3 = sb("h2w3", [P, H])
        mlp_out = sb("mlp_out", [P, 1])
        fsum = sb("fsum", [P, R])
        fsum_sq = sb("fsum_sq", [P, D])
        ssq = sb("ssq", [P, 1])
        sq_all = sb("sq_all", [P, F, D])
        sq = sb("sq", [P, 1])
        fm2 = sb("fm2", [P, 1])
        lin_fm = sb("lin_fm", [P, 1])
        partial = sb("partial", [P, 1])
        bias3 = sb("bias3", [P, 3])
        bias = sb("bias", [P, 1])
        y = sb("y", [P, T])
        ident = sb("ident", [P, P])
        ones = sb("ones", [P, 1])

        ps_t = [psum("ps_t0"), psum("ps_t1")]
        ps_last = [psum("ps_last0"), psum("ps_last1")]
        ps_q = [psum("ps_q0"), psum("ps_q1")]
        ps_mlp = psum("ps_mlp")
        ps_y = psum("ps_y")

        idx_in, ix_step, base_ready = sem("idx_in"), sem("ix_step"), sem("base_ready")
        ident_zero, ident_ready, const_ready = sem("ident_zero"), sem("ident_ready"), sem("const_ready")
        w2_in, w1_in, w0_in = sem("w2_in"), sem("w1_in"), sem("w0_in")
        lin_in, m1_in, m2_in, small_in = sem("lin_in"), sem("m1_in"), sem("m2_in"), sem("small_in")
        m_done, m_copied, b_done, b_copied = sem("m_done"), sem("m_copied"), sem("b_done"), sem("b_copied")
        zw_step = [sem("zw_last_step"), sem("zw_q_step")]
        zw_filled = [6, 7]
        zwt_done = sem("zwt_done")
        zw_hi_ready, zw_lo_ready = sem("zw_hi_ready"), sem("zw_lo_ready")
        m_hi_ready, m_lo_ready, bias_ready = sem("m_hi_ready"), sem("m_lo_ready"), sem("bias_ready")
        gather_ready = [sem(f"gather_ready{b}") for b in range(BUF)]
        gathered = [sem(f"gathered{b}") for b in range(BUF)]
        by_pos_ready = sem("by_pos_ready")
        fields_doubled, z_fields, z_pairs = sem("fields_doubled"), sem("z_fields"), sem("z_pairs")
        zt_done, z_hi_ready, z_lo_ready = sem("zt_done"), sem("z_hi_ready"), sem("z_lo_ready")
        quad_done, last_copied, prod_ready, y_done = sem("quad_done"), sem("last_copied"), sem("prod_ready"), sem("y_done")
        embt_done, embt_hi_ready, embt_lo_ready = sem("embt_done"), sem("embt_hi_ready"), sem("embt_lo_ready")
        h1_done, h1_ready, h1t_done = sem("h1_done"), sem("h1_ready"), sem("h1t_done")
        h1t_hi_ready, h1t_lo_ready = sem("h1t_hi_ready"), sem("h1t_lo_ready")
        h2_done, mlp_bank_free = sem("h2_done"), sem("mlp_bank_free")
        fsum_ready, ssq_ready, sq_ready = sem("fsum_ready"), sem("ssq_ready"), sem("sq_ready")
        fm2_ready, lin_fm_ready, partial_ready = sem("fm2_ready"), sem("lin_fm_ready"), sem("partial_ready")
        tile_ready, out_stored = sem("tile_ready"), sem("out_stored")

        block = ctx.enter_context(nc.Block())

        @block.sync
        def _(sp):
            sp.dma_start(idx_raw[:], x_idx.rearrange("(p t) f -> p t f", t=T)).then_inc(idx_in, 16)
            sp.dma_start(w2[:], cin_w2).then_inc(w2_in, 16)
            sp.dma_start(w1[:], cin_w1).then_inc(w1_in, 16)
            sp.dma_start(w0[:], cin_w0).then_inc(w0_in, 16)
            by_position = mlp_w1.rearrange("(f d) h -> d f h", d=D)
            for c in range(4):
                for j in range(QUAD):
                    sp.dma_start(m1_raw[j * F:(j + 1) * F, c, :], by_position[c * QUAD + j]).then_inc(m1_in, 16)
            sp.dma_start(m1_raw[EC:EC + 1, 3, :], mlp_b1.rearrange("(o h) -> o h", o=1)).then_inc(m1_in, 16)
            sp.dma_start(m2_raw[0:HC, :, :], mlp_w2.rearrange("(c k) h -> k c h", k=HC)).then_inc(m2_in, 16)
            sp.dma_start(m2_raw[HC:HC + 1, 3, :], mlp_b2.rearrange("(o h) -> o h", o=1)).then_inc(m2_in, 16)
            sp.wait_ge(tile_ready, T)
            sp.dma_start(out.rearrange("(p t) o -> p (t o)", t=T), y[:]).then_inc(out_stored, 16)
            sp.wait_ge(out_stored, 16)

        @block.gpsimd
        def _(pool):
            pool.iota(row_base[:], pattern=[[V, F]], base=0, channel_multiplier=0).then_inc(base_ready, 1)
            pool.memset(ident[:], 0.0).then_inc(ident_zero, 1)
            pool.wait_ge(ident_zero, 1)
            pool.affine_select(out=ident[:], in_=ident[:], compare_op=ALU.not_equal, fill=1.0, base=0,
                               pattern=[[-1, P]], channel_multiplier=1).then_inc(ident_ready, 1)
            with pool.Fori(1, T // BUF + 1) as turn:
                for b in range(BUF):
                    pool.wait_ge(ix_step, 5)
                    pool.wait_ge(gather_ready[b], turn)
                    for f in range(F):
                        pool.indirect_dma_start(emb[b][:, f, :], None, rows,
                                                bass.IndirectOffsetOnAxis(ix_now[b][:, f:f + 1], 0)
                                                ).then_inc(gathered[b], 16)

        @block.scalar
        def _(act):
            for c in range(3):
                act.dma_start(lin[:, c:c + 1], lin_w[c * K:(c + 1) * K, :]).then_inc(lin_in, 16)
            act.dma_start(w3_all[:], mlp_w3.rearrange("h o -> (o h)").partition_broadcast(P)).then_inc(small_in, 16)
            for c, v in enumerate((w1_bias, mlp_b3, lin_b)):
                act.dma_start(bias3[:, c:c + 1], v.partition_broadcast(P)).then_inc(small_in, 16)
            act.wait_ge(lin_in, 16 * 3)
            act.activation(m_lin2[:, F:F + 1], lin[:, 1:2], ACT.Copy).then_inc(m_copied, 1)
            act.wait_ge(m_done, 1)
            act.activation(m_lin2[:, 0:F], ps_y[:, 0:F], ACT.Copy).then_inc(m_copied, 1)
            act.wait_ge(m1_in, 16 * (D + 1))
            act.activation(m1_hi[0:EC, 0:3, :], m1_raw[0:EC, 0:3, :], ACT.Copy).then_inc(m_hi_ready, 1)
            act.activation(m1_hi[0:EC + 1, 3, :], m1_raw[0:EC + 1, 3, :], ACT.Copy).then_inc(m_hi_ready, 1)
            act.wait_ge(m2_in, 16 * 2)
            act.activation(m2_hi[0:HC, 0:3, :], m2_raw[0:HC, 0:3, :], ACT.Copy).then_inc(m_hi_ready, 1)
            act.activation(m2_hi[0:HC + 1, 3, :], m2_raw[0:HC + 1, 3, :], ACT.Copy).then_inc(m_hi_ready, 1)
            act.wait_ge(b_done, 1)
            for h in range(2):
                act.activation(b_a[:, HALF * h:HALF * (h + 1), :],
                               ps_q[h][:, 0:HALF * (F + 1)].rearrange("p (f g) -> p f g", g=F + 1),
                               ACT.Copy).then_inc(b_copied, 1)
            for o in (LAST, Q):
                act.wait_ge(zwt_done, o + 1)
                act.activation(zw_hi[0:ZC, o], ps_t[o][0:ZC, 0:NC * P].rearrange("p (c l) -> p c l", c=NC),
                               ACT.Copy).then_inc(zw_hi_ready, 1)

            with act.Fori(0, T // BUF) as i:
                for b in range(BUF):
                    t = i * BUF + b
                    e = emb[b]
                    act.wait_ge(gathered[b], (i + 1) * 16 * F)
                    act.activation(by_pos[:].rearrange("p (d f) -> p d f", f=F), e[:, 0:F, 0:D].rearrange("p f d -> p d f"),
                                   ACT.Copy).then_inc(by_pos_ready, 1)
                    act.activation(e[:, F:F + HALF, 0:D], e[:, 0:HALF, 0:D], ACT.Copy).then_inc(fields_doubled, 1)
                    act.activation(z[:, :, NPAIR:NPAIR + F], e[:, 0:F, 0:D].rearrange("p f d -> p d f"),
                                   ACT.Copy).then_inc(z_fields, 1)

                    def embt_high():
                        act.wait_ge(embt_done, t + 1)
                        v = ps_mlp[:].rearrange("p (c n) -> p c n", c=4)
                        act.activation(embt_hi[0:EC], v[0:EC], ACT.Copy).then_inc(embt_hi_ready, 1)

                    def z_high(u):
                        act.wait_ge(zt_done, t * NU + u + 1)
                        act.activation(z_hi[0:ZC, u % 2, :], ps_t[u % 2][0:ZC, :], ACT.Copy).then_inc(z_hi_ready, 1)

                    def copy_last(q):
                        act.wait_ge(quad_done, t * NQ + q + 1)
                        act.activation(last_sb[:, q % 2, :], ps_last[q % 2][:], ACT.Copy).then_inc(last_copied, 1)

                    embt_high()
                    for u in range(NU):
                        z_high(u)
                        if u == 0:
                            act.activation(sq_all[:], e[:, 0:F, 0:D], ACT.Square, accum_out=sq[:]).then_inc(sq_ready, 1)
                        if u == 2:
                            act.wait_ge(h1_done, t + 1)
                            act.activation(h1[:], ps_mlp[:, 0:H], ACT.Relu).then_inc(h1_ready, 1)
                        if u == 5:
                            act.wait_ge(h1t_done, t + 1)
                            act.activation(h1t_hi[0:HC], ps_mlp[0:HC, :].rearrange("p (c n) -> p c n", c=4),
                                           ACT.Copy).then_inc(h1t_hi_ready, 1)
                        if u >= 3 and u % 3 == 0:
                            copy_last(u // 3 - 1)
                    copy_last(NQ - 1)

        @block.vector
        def _(dve):
            dve.wait_ge(idx_in, 16)
            dve.tensor_scalar(idx_wrap[:], idx_raw[:], 0.0, float(V), ALU.is_lt, ALU.mult).then_inc(ix_step, 1)
            dve.wait_ge(ix_step, 1)
            dve.tensor_tensor(idx_sum[:], idx_wrap[:], idx_raw[:], ALU.add).then_inc(ix_step, 1)
            dve.wait_ge(ix_step, 2)
            dve.tensor_scalar(idx_wrap[:], idx_sum[:], 0.0, float(V - 1), ALU.max, ALU.min).then_inc(ix_step, 1)
            dve.wait_ge(ix_step, 3)
            dve.wait_ge(base_ready, 1)
            dve.tensor_tensor(row_ix[:, 0:T, :], idx_wrap[:], row_base[:].unsqueeze(1).to_broadcast([P, T, F]),
                              ALU.add).then_inc(ix_step, 1)
            dve.memset(row_ix[:, T:T + BUF, :], 0).then_inc(ix_step, 1)
            dve.wait_ge(ix_step, 5)
            for b in range(BUF):
                dve.tensor_copy(ix_now[b][:], row_ix[:, b, :]).then_inc(gather_ready[b], 1)

            dve.memset(ones[:], 1.0).then_inc(mlp_bank_free, 1)
            dve.memset(z[:, :, ZW - 1:ZW], 1.0).then_inc(const_ready, 1)
            dve.memset(embt_hi[96:EC + 1, 3, :].bitcast(F32), 1.0).then_inc(const_ready, 1)
            dve.memset(h1t_hi[96:HC + 1, 3, :].bitcast(F32), 1.0).then_inc(const_ready, 1)
            dve.memset(zw[LAST][:, NPAIR:ZW], 0.0).then_inc(zw_step[LAST], 1)

            def pair_weights(o, w):
                before = zw_filled[o] - 5
                s = sym[o]
                dve.tensor_tensor(s[:, :, 0:F], w, w.rearrange("p a b -> p b a"), ALU.add).then_inc(zw_step[o], 1)
                dve.wait_ge(zw_step[o], before + 1)
                dve.tensor_copy(s[:, :, F:2 * F], s[:, :, 0:F]).then_inc(zw_step[o], 1)
                dve.wait_ge(zw_step[o], before + 2)
                base = s[:]
                part, diag = list(base.ap)[0], w
                dve.tensor_copy(zw[o][:, F:HALF * F].rearrange("p (s f) -> p s f", f=F),
                                bass.AP(base.tensor, base.offset + 1, [part, [1, HALF - 1], [2 * F + 1, F]])
                                ).then_inc(zw_step[o], 1)
                dve.tensor_copy(zw[o][:, HALF * F:NPAIR],
                                bass.AP(base.tensor, base.offset + HALF, [part, [2 * F + 1, HALF]])).then_inc(zw_step[o], 1)
                row = list(diag.ap)[1][0]
                dve.tensor_copy(zw[o][:, 0:F],
                                bass.AP(diag.tensor, diag.offset, [list(diag.ap)[0], [row + 1, F]])).then_inc(zw_step[o], 1)

            dve.wait_ge(w0_in, 16)
            pair_weights(LAST, w0[:])
            dve.wait_ge(lin_in, 16 * 3)
            dve.tensor_copy(zw[Q][:, ZW - 1:ZW], lin[:, 0:1]).then_inc(zw_step[Q], 1)

            dve.wait_ge(m_hi_ready, 4)
            for hi, lo, raw, part, cs in ((m1_hi, m1_lo, m1_raw, slice(0, EC), slice(0, 3)),
                                          (m1_hi, m1_lo, m1_raw, slice(0, EC + 1), slice(3, 4)),
                                          (m2_hi, m2_lo, m2_raw, slice(0, HC), slice(0, 3)),
                                          (m2_hi, m2_lo, m2_raw, slice(0, HC + 1), slice(3, 4))):
                dve.tensor_tensor(lo[part, cs, :], raw[part, cs, :], hi[part, cs, :].bitcast(F32),
                                  ALU.subtract).then_inc(m_lo_ready, 1)
            dve.wait_ge(small_in, 16 * 4)
            dve.tensor_reduce(bias[:], bias3[:], AX.X, ALU.add).then_inc(bias_ready, 1)

            dve.wait_ge(b_copied, 2)
            dve.tensor_copy(zw[Q][:, NPAIR:NPAIR + F], b_a[:, :, F]).then_inc(zw_step[Q], 1)
            pair_weights(Q, b_a[:, :, 0:F])
            for o in (LAST, Q):
                dve.wait_ge(zw_hi_ready, o + 1)
                dve.tensor_tensor(zw_lo[0:ZC, o], ps_t[o][0:ZC, 0:NC * P].rearrange("p (c l) -> p c l", c=NC),
                                  zw_hi[0:ZC, o].bitcast(F32), ALU.subtract).then_inc(zw_lo_ready, 1)

            with dve.Fori(0, T // BUF) as i:
                for b in range(BUF):
                    t = i * BUF + b
                    e = emb[b][:]
                    part = list(e.ap)[0]

                    def pairs(q):
                        d0 = e.offset + QUAD * q
                        dve.tensor_tensor(
                            z[:, QUAD * q:QUAD * (q + 1), 0:HALF * F].rearrange("p d (s f) -> p d s f", f=F),
                            bass.AP(e.tensor, d0, [part, [1, QUAD], [0, HALF], [R, F]]),
                            bass.AP(e.tensor, d0, [part, [1, QUAD], [R, HALF], [R, F]]), ALU.mult)
                        dve.tensor_tensor(
                            z[:, QUAD * q:QUAD * (q + 1), HALF * F:NPAIR],
                            bass.AP(e.tensor, d0, [part, [1, QUAD], [R, HALF]]),
                            bass.AP(e.tensor, d0 + HALF * R, [part, [1, QUAD], [R, HALF]]),
                            ALU.mult).then_inc(z_pairs, 1)

                    def z_low(u):
                        dve.wait_ge(z_hi_ready, t * NU + u + 1)
                        dve.tensor_tensor(z_lo[0:ZC, u % 2, :], ps_t[u % 2][0:ZC, :],
                                          z_hi[0:ZC, u % 2, :].bitcast(F32), ALU.subtract).then_inc(z_lo_ready, 1)

                    def last_times_q(q):
                        dve.wait_ge(last_copied, t * NQ + q + 1)
                        dve.tensor_tensor(prod[:, q % 2, :], ps_q[q % 2][:], last_sb[:, q % 2, :],
                                          ALU.mult).then_inc(prod_ready, 1)

                    def embt_low():
                        v = ps_mlp[:].rearrange("p (c n) -> p c n", c=4)
                        dve.wait_ge(embt_hi_ready, t + 1)
                        dve.tensor_tensor(embt_lo[0:EC], v[0:EC], embt_hi[0:EC].bitcast(F32),
                                          ALU.subtract).then_inc(embt_lo_ready, 1)

                    def first_order_and_fm():
                        dve.tensor_reduce(fsum[:], emb[b][:, 0:F, :].rearrange("p f r -> p r f"), AX.X,
                                          ALU.add).then_inc(fsum_ready, 1)
                        dve.wait_ge(fsum_ready, t + 1)
                        dve.tensor_tensor_reduce(fsum_sq[:], fsum[:, 0:D], fsum[:, 0:D], 1.0, 0.0, ALU.mult, ALU.add,
                                                 ssq[:]).then_inc(ssq_ready, 1)
                        dve.wait_ge(ssq_ready, t + 1)
                        dve.wait_ge(sq_ready, t + 1)
                        dve.tensor_tensor(fm2[:], ssq[:], sq[:], ALU.subtract).then_inc(fm2_ready, 1)
                        dve.wait_ge(fm2_ready, t + 1)
                        dve.scalar_tensor_tensor(lin_fm[:], fm2[:], 0.5, fsum[:, D:R], ALU.mult,
                                                 ALU.add).then_inc(lin_fm_ready, 1)

                    dve.wait_ge(gathered[b], (i + 1) * 16 * F)
                    dve.wait_ge(fields_doubled, t + 1)
                    pairs(0)
                    embt_low()
                    pairs(1)
                    for u in range(NU):
                        z_low(u)
                        if u == 2:
                            pairs(2)
                        if u == 5:
                            dve.wait_ge(h1t_hi_ready, t + 1)
                            dve.tensor_tensor(h1t_lo[0:HC], ps_mlp[0:HC, :].rearrange("p (c n) -> p c n", c=4),
                                              h1t_hi[0:HC].bitcast(F32), ALU.subtract).then_inc(h1t_lo_ready, 1)
                            pairs(3)
                        if u >= 3 and u % 3 == 0:
                            last_times_q(u // 3 - 1)
                        if u == 7:
                            first_order_and_fm()
                            dve.tensor_copy(ix_now[b][:], row_ix[:, t + BUF, :]).then_inc(gather_ready[b], 1)
                    last_times_q(NQ - 1)
                    dve.wait_ge(h2_done, t + 1)
                    dve.scalar_tensor_tensor(h2w3[:], ps_mlp[:, 0:H], 0.0, w3_all[:], ALU.max, ALU.mult,
                                             accum_out=mlp_out[:]).then_inc(mlp_bank_free, 1)
                    dve.wait_ge(mlp_bank_free, t + 2)
                    dve.scalar_tensor_tensor(partial[:], mlp_out[:], bias[:, 0:1], lin_fm[:], ALU.add,
                                             ALU.add).then_inc(partial_ready, 1)
                    dve.wait_ge(partial_ready, t + 1)
                    dve.wait_ge(y_done, t + 1)
                    dve.tensor_tensor(y[:, bass.ds(t, 1)], ps_y[:, 0:1], partial[:], ALU.add).then_inc(tile_ready, 1)

        @block.tensor
        def _(pe):
            pe.wait_ge(w2_in, 16)
            pe.wait_ge(lin_in, 16 * 3)
            for g in range(F):
                mm = pe.matmul(ps_y[:, g:g + 1], w2[:, :, g], lin[:, 2:3], start=True, stop=True)
            mm.then_inc(m_done, 1)
            pe.wait_ge(w1_in, 16)
            pe.wait_ge(m_copied, 2)
            for f in range(F):
                c = (f % HALF) * (F + 1)
                mm = pe.matmul(ps_q[f // HALF][:, c:c + F + 1], w1[:, :, f], m_lin2[:], start=True, stop=True)
            mm.then_inc(b_done, 1)
            pe.wait_ge(ident_ready, 1)
            for o in (LAST, Q):
                pe.wait_ge(zw_step[o], zw_filled[o])
                for c in range(NC):
                    mm = pe.transpose(ps_t[o][0:ZC, c * P:(c + 1) * P], zw[o][:, c * ZC:(c + 1) * ZC], ident[:])
                mm.then_inc(zwt_done, 1)
            pe.wait_ge(m_hi_ready, 4)
            pe.wait_ge(m_lo_ready, 4)
            pe.wait_ge(zw_lo_ready, 2)
            pe.wait_ge(const_ready, 3)

            with pe.Fori(0, T // BUF) as i:
                for b in range(BUF):
                    t = i * BUF + b

                    def embt():
                        pe.wait_ge(mlp_bank_free, t + 1)
                        pe.wait_ge(by_pos_ready, t + 1)
                        for c in range(4):
                            mm = pe.transpose(ps_mlp[0:EC, c * P:(c + 1) * P], by_pos[:, c * EC:(c + 1) * EC], ident[:])
                        mm.then_inc(embt_done, 1)

                    def zt(u):
                        q, c = divmod(u, NC)
                        if c == 0:
                            pe.wait_ge(z_pairs, t * NQ + q + 1)
                        if u == 2:
                            pe.wait_ge(z_fields, t + 1)
                        for j in range(QUAD):
                            mm = pe.transpose(ps_t[u % 2][0:ZC, j * P:(j + 1) * P],
                                              z[:, QUAD * q + j, c * ZC:(c + 1) * ZC], ident[:])
                        mm.then_inc(zt_done, 1)

                    def split_matmul(ps, hi_w, lo_w, hi_x, lo_x, first, last):
                        pe.matmul(ps, hi_w, lo_x, start=first, stop=False)
                        pe.matmul(ps, lo_w, hi_x, start=False, stop=False)
                        return pe.matmul(ps, hi_w, hi_x, start=False, stop=last)

                    def main(u):
                        q, c = divmod(u, NC)
                        pe.wait_ge(z_lo_ready, t * NU + u + 1)
                        for o, ps in ((LAST, ps_last), (Q, ps_q)):
                            mm = split_matmul(ps[q % 2][:], zw_hi[0:ZC, o, c], zw_lo[0:ZC, o, c],
                                              z_hi[0:ZC, u % 2, :], z_lo[0:ZC, u % 2, :], c == 0, c == NC - 1)
                        if c == NC - 1:
                            mm.then_inc(quad_done, 1)

                    def sum_prod(q):
                        pe.wait_ge(prod_ready, t * NQ + q + 1)
                        for j in range(QUAD):
                            mm = pe.matmul(ps_y[:, 0:1], prod[:, q % 2, j * P:(j + 1) * P], ones[:],
                                           start=(q == 0 and j == 0), stop=(q == NQ - 1 and j == QUAD - 1))
                        if q == NQ - 1:
                            mm.then_inc(y_done, 1)

                    def hidden1():
                        pe.wait_ge(embt_lo_ready, t + 1)
                        for c in range(4):
                            k = EC
                            pe.matmul(ps_mlp[:, 0:H], embt_lo[0:k, c, :], m1_hi[0:k, c, :], start=(c == 0), stop=False)
                            k += c == 3
                            pe.matmul(ps_mlp[:, 0:H], embt_hi[0:k, c, :], m1_lo[0:k, c, :], start=False, stop=False)
                            mm = pe.matmul(ps_mlp[:, 0:H], embt_hi[0:k, c, :], m1_hi[0:k, c, :], start=False,
                                           stop=(c == 3))
                        mm.then_inc(h1_done, 1)

                    def h1t():
                        pe.wait_ge(h1_ready, t + 1)
                        for c in range(4):
                            mm = pe.transpose(ps_mlp[0:HC, c * P:(c + 1) * P], h1[:, c * HC:(c + 1) * HC], ident[:])
                        mm.then_inc(h1t_done, 1)

                    def hidden2():
                        pe.wait_ge(h1t_lo_ready, t + 1)
                        for c in range(4):
                            k = HC
                            pe.matmul(ps_mlp[:, 0:H], h1t_lo[0:k, c, :], m2_hi[0:k, c, :], start=(c == 0), stop=False)
                            k += c == 3
                            pe.matmul(ps_mlp[:, 0:H], h1t_hi[0:k, c, :], m2_lo[0:k, c, :], start=False, stop=False)
                            mm = pe.matmul(ps_mlp[:, 0:H], h1t_hi[0:k, c, :], m2_hi[0:k, c, :], start=False,
                                           stop=(c == 3))
                        mm.then_inc(h2_done, 1)

                    embt()
                    zt(0)
                    zt(1)
                    for u in range(NU):
                        main(u)
                        if u + 2 < NU:
                            if u == 0:
                                zt(2)
                                hidden1()
                            elif u == 3:
                                zt(5)
                                h1t()
                            else:
                                zt(u + 2)
                        if u >= 3 and u % 3 == 1:
                            sum_prod(u // 3 - 1)
                    hidden2()
                    sum_prod(NQ - 1)


def kernel(**inputs):
    import numpy as np
    import concourse.bacc as bacc
    from concourse.bass_utils import run_bass_kernel_spmd

    nc = bacc.Bacc("TRN2", target_bir_lowering=False, num_devices=1)
    emb = np.ascontiguousarray(inputs["L0_rec_embed_table"])
    first = np.ascontiguousarray(inputs["L0_rec_w1_table"])
    fields, vocab, dim = emb.shape
    arrays = {"x_idx": np.ascontiguousarray(inputs["r_x_idx"]),
              "rows": np.concatenate([emb.reshape(fields * vocab, dim), first.reshape(fields * vocab, 1)], axis=1)}
    for name in ("w1_bias", "mlp_w1", "mlp_b1", "mlp_w2", "mlp_b2", "mlp_w3", "mlp_b3",
                 "cin_w0", "cin_w1", "cin_w2", "lin_w", "lin_b"):
        arrays[name] = np.ascontiguousarray(inputs["L0_rec_" + name])
    args = [nc.dram_tensor(k, a.shape, mybir.dt.from_np(a.dtype), kind="ExternalInput").ap() for k, a in arrays.items()]
    out = nc.dram_tensor("out", (arrays["x_idx"].shape[0], 1), F32, kind="ExternalOutput").ap()
    deepfm_cin_kernel(nc, *args, out)
    return run_bass_kernel_spmd(nc, [arrays], core_ids=[0]).results[0]["out"]
```

```python
from contextlib import ExitStack

import concourse.bass as bass
from concourse import mybir

F32 = mybir.dt.float32
F32R = mybir.dt.float32r
I32 = mybir.dt.int32
ALU = mybir.AluOpType
ACT = mybir.ActivationFunctionType
AX = mybir.AxisListType

P = 128
BANK = 512
QUAD = BANK // P


def deepfm_cin_kernel(nc, x_idx, rows, w1_bias, mlp_w1, mlp_b1, mlp_w2, mlp_b2, mlp_w3, mlp_b3,
                      cin_w0, cin_w1, cin_w2, lin_w, lin_b, out):
    N, F = x_idx.shape
    R = rows.shape[1]
    D = R - 1
    V = rows.shape[0] // F
    K = cin_w0.shape[0]
    H = mlp_w1.shape[1]
    T = N // P
    BUF = 2
    NQ = D // QUAD
    HALF = F // 2
    NPAIR = F * (F + 1) // 2
    ZW = NPAIR + F + 1
    NC = 3
    ZC = ZW // NC
    NU = NQ * NC
    EC = F * D // 4
    HC = H // 4
    LAST, Q = 0, 1
    assert K == P and ZC * NC == ZW and ZC <= P and N % (P * BUF) == 0

    with ExitStack() as ctx:
        def sb(name, shape, dt=F32):
            return ctx.enter_context(nc.sbuf_tensor(name, shape, dt))

        def psum(name):
            return ctx.enter_context(nc.psum_tensor(name, [P, BANK], F32))

        def sem(name):
            return ctx.enter_context(nc.semaphore(name))

        idx_raw = sb("idx_raw", [P, T, F], I32)
        idx_wrap = sb("idx_wrap", [P, T, F])
        idx_sum = sb("idx_sum", [P, T, F])
        idx_clip = sb("idx_clip", [P, T, F])
        row_base = sb("row_base", [P, F], I32)
        row_ix = sb("row_ix", [P, T + BUF, F], I32)
        ix_now = [sb(f"ix_now{b}", [P, F], I32) for b in range(BUF)]
        emb = [sb(f"emb{b}", [P, F + HALF, R]) for b in range(BUF)]
        z = sb("z", [P, D, ZW])
        z_hi = sb("z_hi", [P, NC, BANK], F32R)
        z_lo = sb("z_lo", [P, NC, BANK], F32R)
        last_sb = sb("last_sb", [P, 2, BANK])
        prod = sb("prod", [P, BANK])
        prod_sum = sb("prod_sum", [P, BANK])
        w0 = sb("w0", [P, F, F])
        w1 = sb("w1", [P, K, F])
        w2 = sb("w2", [P, K, F])
        lin = sb("lin", [P, 3])
        m_lin2 = sb("m_lin2", [P, F + 1])
        b_a = sb("b_a", [P, F, F + 1])
        sym = [sb("sym_w0", [P, F, 2 * F]), sb("sym_b", [P, F, 2 * F])]
        zw = [sb("zw_last", [P, ZW]), sb("zw_q", [P, ZW])]
        zw_hi = sb("zw_hi", [P, 2, NC, P], F32R)
        zw_lo = sb("zw_lo", [P, 2, NC, P], F32R)
        m1_raw = sb("m1_raw", [P, 4, H])
        m1_hi = sb("m1_hi", [P, 4, H], F32R)
        m1_lo = sb("m1_lo", [P, 4, H], F32R)
        m2_raw = sb("m2_raw", [P, 4, H])
        m2_hi = sb("m2_hi", [P, 4, H], F32R)
        m2_lo = sb("m2_lo", [P, 4, H], F32R)
        w3_all = sb("w3_all", [P, H])
        by_pos = sb("by_pos", [P, D * F])
        embt_hi = sb("embt_hi", [P, 4, P], F32R)
        embt_lo = sb("embt_lo", [P, 4, P], F32R)
        h1 = sb("h1", [P, H])
        h1t_hi = sb("h1t_hi", [P, 4, P], F32R)
        h1t_lo = sb("h1t_lo", [P, 4, P], F32R)
        h2w3 = sb("h2w3", [P, H])
        mlp_out = sb("mlp_out", [P, 1])
        fsum = sb("fsum", [P, R])
        fsum_sq = sb("fsum_sq", [P, D])
        ssq = sb("ssq", [P, 1])
        sq_all = sb("sq_all", [P, F, D])
        sq = sb("sq", [P, 1])
        fm2 = sb("fm2", [P, 1])
        lin_fm = sb("lin_fm", [P, 1])
        partial = sb("partial", [P, 1])
        bias3 = sb("bias3", [P, 3])
        bias = sb("bias", [P, 1])
        y = sb("y", [P, T])
        ident = sb("ident", [P, P])
        ones = sb("ones", [P, 1])

        ps_t = [psum(f"ps_t{c}") for c in range(NC)]
        ps_last = psum("ps_last")
        ps_q = [psum("ps_q0"), psum("ps_q1")]
        ps_mlp = psum("ps_mlp")
        ps_y = psum("ps_y")

        idx_in, ix_step, base_ready = sem("idx_in"), sem("ix_step"), sem("base_ready")
        ident_zero, ident_ready, const_ready = sem("ident_zero"), sem("ident_ready"), sem("const_ready")
        w2_in, w1_in, w0_in = sem("w2_in"), sem("w1_in"), sem("w0_in")
        lin_in, m1_in, m2_in, small_in = sem("lin_in"), sem("m1_in"), sem("m2_in"), sem("small_in")
        m_done, m_copied, b_done, b_copied = sem("m_done"), sem("m_copied"), sem("b_done"), sem("b_copied")
        zw_step = [sem("zw_last_step"), sem("zw_q_step")]
        ps_zw = [ps_last, ps_mlp]
        zw_filled = [6, 7]
        zwt_done = sem("zwt_done")
        zw_hi_ready, zw_lo_ready = sem("zw_hi_ready"), sem("zw_lo_ready")
        m_hi_ready, m_lo_ready, bias_ready = sem("m_hi_ready"), sem("m_lo_ready"), sem("bias_ready")
        gather_ready = [sem(f"gather_ready{b}") for b in range(BUF)]
        gathered = [sem(f"gathered{b}") for b in range(BUF)]
        by_pos_ready = sem("by_pos_ready")
        fields_doubled, z_fields, z_pairs = sem("fields_doubled"), sem("z_fields"), sem("z_pairs")
        zt_done, z_hi_ready, z_lo_ready = sem("zt_done"), sem("z_hi_ready"), sem("z_lo_ready")
        quad_done, last_bank_free, prod_ready = sem("quad_done"), sem("last_bank_free"), sem("prod_ready")
        prod_added, y_done = sem("prod_added"), sem("y_done")
        embt_done, embt_hi_ready, embt_lo_ready = sem("embt_done"), sem("embt_hi_ready"), sem("embt_lo_ready")
        h1_done, h1_ready, h1t_done = sem("h1_done"), sem("h1_ready"), sem("h1t_done")
        h1t_hi_ready, h1t_lo_ready = sem("h1t_hi_ready"), sem("h1t_lo_ready")
        h2_done, mlp_bank_free = sem("h2_done"), sem("mlp_bank_free")
        fsum_ready, ssq_ready, sq_ready = sem("fsum_ready"), sem("ssq_ready"), sem("sq_ready")
        fm2_ready, lin_fm_ready, partial_ready = sem("fm2_ready"), sem("lin_fm_ready"), sem("partial_ready")
        tile_ready, out_stored = sem("tile_ready"), sem("out_stored")

        def run_tiles(engine, between, tile):
            with engine.Fori(0, T // BUF - 1) as i:
                tile(i * 2, 0)
                between(i * 2, i * 2 + 1, i + 1, 1)
                tile(i * 2 + 1, 1)
                between(i * 2 + 1, i * 2 + 2, i + 2, 0)
            tile(T - 2, 0)
            between(T - 2, T - 1, T // BUF, 1)
            tile(T - 1, 1)
            between(T - 1, None, None, None)

        block = ctx.enter_context(nc.Block())

        @block.sync
        def _(sp):
            sp.dma_start(idx_raw[:], x_idx.rearrange("(p t) f -> p t f", t=T)).then_inc(idx_in, 16)
            for c in (2, 1, 0):
                sp.dma_start(lin[:, c:c + 1], lin_w[c * K:(c + 1) * K, :]).then_inc(lin_in, 16)
            sp.dma_start(w1[:], cin_w1).then_inc(w1_in, 16)
            sp.dma_start(w0[:], cin_w0).then_inc(w0_in, 16)
            sp.dma_start(m1_raw[0:EC, :, :], mlp_w1.rearrange("(c k) h -> k c h", k=EC)).then_inc(m1_in, 16)
            sp.dma_start(m1_raw[EC:EC + 1, 3, :], mlp_b1.rearrange("(o h) -> o h", o=1)).then_inc(m1_in, 16)
            sp.dma_start(m2_raw[0:HC, :, :], mlp_w2.rearrange("(c k) h -> k c h", k=HC)).then_inc(m2_in, 16)
            sp.dma_start(m2_raw[HC:HC + 1, 3, :], mlp_b2.rearrange("(o h) -> o h", o=1)).then_inc(m2_in, 16)
            sp.wait_ge(tile_ready, T)
            sp.dma_start(out.rearrange("(p t) o -> p (t o)", t=T), y[:]).then_inc(out_stored, 16)
            sp.wait_ge(out_stored, 16)

        @block.gpsimd
        def _(pool):
            pool.iota(row_base[:], pattern=[[V, F]], base=0, channel_multiplier=0).then_inc(base_ready, 1)
            pool.memset(ident[:], 0.0).then_inc(ident_zero, 1)
            pool.wait_ge(ident_zero, 1)
            pool.affine_select(out=ident[:], in_=ident[:], compare_op=ALU.not_equal, fill=1.0, base=0,
                               pattern=[[-1, P]], channel_multiplier=1).then_inc(ident_ready, 1)
            with pool.Fori(1, T // BUF + 1) as turn:
                for b in range(BUF):
                    pool.wait_ge(ix_step, 4)
                    pool.wait_ge(gather_ready[b], turn)
                    for f in range(F):
                        pool.indirect_dma_start(emb[b][:, f, :], None, rows,
                                                bass.IndirectOffsetOnAxis(ix_now[b][:, f:f + 1], 0)
                                                ).then_inc(gathered[b], 16)

        @block.scalar
        def _(act):
            act.dma_start(w2[:], cin_w2).then_inc(w2_in, 16)
            act.dma_start(w3_all[:], mlp_w3.rearrange("h o -> (o h)").partition_broadcast(P)).then_inc(small_in, 16)
            for c, v in enumerate((w1_bias, mlp_b3, lin_b)):
                act.dma_start(bias3[:, c:c + 1], v.partition_broadcast(P)).then_inc(small_in, 16)
            act.wait_ge(lin_in, 16 * 3)
            act.activation(m_lin2[:, F:F + 1], lin[:, 1:2], ACT.Copy).then_inc(m_copied, 1)
            act.wait_ge(m1_in, 16 * 2)
            act.activation(m1_hi[0:EC, 0:3, :], m1_raw[0:EC, 0:3, :], ACT.Copy).then_inc(m_hi_ready, 1)
            act.activation(m1_hi[0:EC + 1, 3, :], m1_raw[0:EC + 1, 3, :], ACT.Copy).then_inc(m_hi_ready, 1)
            act.wait_ge(m2_in, 16 * 2)
            act.activation(m2_hi[0:HC, 0:3, :], m2_raw[0:HC, 0:3, :], ACT.Copy).then_inc(m_hi_ready, 1)
            act.activation(m2_hi[0:HC + 1, 3, :], m2_raw[0:HC + 1, 3, :], ACT.Copy).then_inc(m_hi_ready, 1)
            act.wait_ge(m_done, 1)
            act.activation(m_lin2[:, 0:F], ps_y[:, 0:F], ACT.Copy).then_inc(m_copied, 1)
            def zw_high(o):
                act.wait_ge(zwt_done, o + 1)
                act.activation(zw_hi[0:ZC, o], ps_zw[o][0:ZC, 0:NC * P].rearrange("p (c l) -> p c l", c=NC),
                               ACT.Copy).then_inc(zw_hi_ready, 1)

            def start_tile(t, turn, b):
                act.wait_ge(gathered[b], turn * 16 * F)
                act.activation(emb[b][:, F:F + HALF, 0:D], emb[b][:, 0:HALF, 0:D], ACT.Copy).then_inc(fields_doubled, 1)
                act.activation(z[:, :, NPAIR:NPAIR + F], emb[b][:, 0:F, 0:D].rearrange("p f d -> p d f"),
                               ACT.Copy).then_inc(z_fields, 1)

            def copy_by_position(b):
                act.activation(by_pos[:].rearrange("p (d f) -> p d f", f=F),
                               emb[b][:, 0:F, 0:D].rearrange("p f d -> p d f"), ACT.Copy).then_inc(by_pos_ready, 1)

            def z_high(t, u):
                act.wait_ge(zt_done, t * NU + u + 1)
                act.activation(z_hi[0:ZC, u % NC, :], ps_t[u % NC][0:ZC, :], ACT.Copy).then_inc(z_hi_ready, 1)

            def copy_last(t, q):
                act.wait_ge(quad_done, t * NQ + q + 1)
                act.activation(last_sb[:, q % 2, :], ps_last[:], ACT.Copy).then_inc(last_bank_free, 1)

            def between(t, after, turn, b):
                if after is not None:
                    start_tile(after, turn, b)
                copy_last(t, NQ - 1)
                if after is not None:
                    z_high(after, 0)
                    z_high(after, 1)
                    copy_by_position(b)
                    z_high(after, 2)

            def tile(t, b):
                for u in range(NC, NU):
                    z_high(t, u)
                    if u == 3:
                        act.wait_ge(embt_done, t + 1)
                        act.activation(embt_hi[0:EC], ps_mlp[0:EC, :].rearrange("p (c n) -> p c n", c=4),
                                       ACT.Copy).then_inc(embt_hi_ready, 1)
                    if u == 5:
                        act.wait_ge(h1_done, t + 1)
                        act.activation(h1[:], ps_mlp[:, 0:H], ACT.Relu).then_inc(h1_ready, 1)
                    if u == 6:
                        act.activation(sq_all[:], emb[b][:, 0:F, 0:D], ACT.Square, accum_out=sq[:]).then_inc(sq_ready, 1)
                    if u == 8:
                        act.wait_ge(h1t_done, t + 1)
                        act.activation(h1t_hi[0:HC], ps_mlp[0:HC, :].rearrange("p (c n) -> p c n", c=4),
                                       ACT.Copy).then_inc(h1t_hi_ready, 1)
                    if u % NC == 1:
                        copy_last(t, u // NC - 1)

            start_tile(0, 1, 0)
            act.wait_ge(b_done, 1)
            for h in range(2):
                act.activation(b_a[:, HALF * h:HALF * (h + 1), :],
                               ps_q[h][:, 0:HALF * (F + 1)].rearrange("p (f g) -> p f g", g=F + 1),
                               ACT.Copy).then_inc(b_copied, 1)
            zw_high(LAST)
            z_high(0, 0)
            z_high(0, 1)
            zw_high(Q)
            copy_by_position(0)
            z_high(0, 2)
            run_tiles(act, between, tile)

        @block.vector
        def _(dve):
            dve.wait_ge(idx_in, 16)
            done = 0
            for ts in (slice(0, 1), slice(1, T)):
                n = ts.stop - ts.start
                dve.tensor_scalar(idx_wrap[:, ts], idx_raw[:, ts], 0.0, float(V), ALU.is_lt, ALU.mult).then_inc(ix_step, 1)
                dve.wait_ge(ix_step, done + 1)
                dve.tensor_tensor(idx_sum[:, ts], idx_wrap[:, ts], idx_raw[:, ts], ALU.add).then_inc(ix_step, 1)
                dve.wait_ge(ix_step, done + 2)
                dve.tensor_scalar(idx_clip[:, ts], idx_sum[:, ts], 0.0, float(V - 1), ALU.max, ALU.min).then_inc(ix_step, 1)
                dve.wait_ge(ix_step, done + 3)
                dve.wait_ge(base_ready, 1)
                dve.tensor_tensor(row_ix[:, ts], idx_clip[:, ts], row_base[:].unsqueeze(1).to_broadcast([P, n, F]),
                                  ALU.add).then_inc(ix_step, 1)
                done += 4
                dve.wait_ge(ix_step, done)
                dve.tensor_copy(ix_now[ts.start][:], row_ix[:, ts.start]).then_inc(gather_ready[ts.start], 1)
            dve.memset(row_ix[:, T:T + BUF, :], 0).then_inc(const_ready, 1)

            dve.memset(ones[:], 1.0).then_inc(mlp_bank_free, 1)
            dve.memset(z[:, :, ZW - 1:ZW], 1.0).then_inc(last_bank_free, 1)
            dve.memset(embt_hi[96:EC + 1, 3, :].bitcast(F32), 1.0).then_inc(const_ready, 1)
            dve.memset(h1t_hi[96:HC + 1, 3, :].bitcast(F32), 1.0).then_inc(const_ready, 1)
            dve.memset(zw[LAST][:, NPAIR:ZW], 0.0).then_inc(zw_step[LAST], 1)

            def pair_weights(o, w):
                before = zw_filled[o] - 5
                s = sym[o]
                dve.tensor_tensor(s[:, :, 0:F], w, w.rearrange("p a b -> p b a"), ALU.add).then_inc(zw_step[o], 1)
                dve.wait_ge(zw_step[o], before + 1)
                dve.tensor_copy(s[:, :, F:2 * F], s[:, :, 0:F]).then_inc(zw_step[o], 1)
                dve.wait_ge(zw_step[o], before + 2)
                base = s[:]
                part, diag = list(base.ap)[0], w
                dve.tensor_copy(zw[o][:, F:HALF * F].rearrange("p (s f) -> p s f", f=F),
                                bass.AP(base.tensor, base.offset + 1, [part, [1, HALF - 1], [2 * F + 1, F]])
                                ).then_inc(zw_step[o], 1)
                dve.tensor_copy(zw[o][:, HALF * F:NPAIR],
                                bass.AP(base.tensor, base.offset + HALF, [part, [2 * F + 1, HALF]])).then_inc(zw_step[o], 1)
                row = list(diag.ap)[1][0]
                dve.tensor_copy(zw[o][:, 0:F],
                                bass.AP(diag.tensor, diag.offset, [list(diag.ap)[0], [row + 1, F]])).then_inc(zw_step[o], 1)

            dve.wait_ge(w0_in, 16)
            pair_weights(LAST, w0[:])
            dve.wait_ge(lin_in, 16 * 3)
            dve.tensor_copy(zw[Q][:, ZW - 1:ZW], lin[:, 0:1]).then_inc(zw_step[Q], 1)

            dve.wait_ge(m_hi_ready, 4)
            for hi, lo, raw, part, cs in ((m1_hi, m1_lo, m1_raw, slice(0, EC), slice(0, 3)),
                                          (m1_hi, m1_lo, m1_raw, slice(0, EC + 1), slice(3, 4)),
                                          (m2_hi, m2_lo, m2_raw, slice(0, HC), slice(0, 3)),
                                          (m2_hi, m2_lo, m2_raw, slice(0, HC + 1), slice(3, 4))):
                dve.tensor_tensor(lo[part, cs, :], raw[part, cs, :], hi[part, cs, :].bitcast(F32),
                                  ALU.subtract).then_inc(m_lo_ready, 1)
            dve.wait_ge(small_in, 16 * 4)
            dve.tensor_reduce(bias[:], bias3[:], AX.X, ALU.add).then_inc(bias_ready, 1)

            def zw_low(o):
                dve.wait_ge(zw_hi_ready, o + 1)
                dve.tensor_tensor(zw_lo[0:ZC, o], ps_zw[o][0:ZC, 0:NC * P].rearrange("p (c l) -> p c l", c=NC),
                                  zw_hi[0:ZC, o].bitcast(F32), ALU.subtract).then_inc(zw_lo_ready, 1)

            def pairs(t, b, q):
                e = emb[b][:]
                part, d0 = list(e.ap)[0], e.offset + QUAD * q
                if q == 0:
                    dve.wait_ge(fields_doubled, t + 1)
                dve.tensor_tensor(
                    z[:, QUAD * q:QUAD * (q + 1), 0:HALF * F].rearrange("p d (s f) -> p d s f", f=F),
                    bass.AP(e.tensor, d0, [part, [1, QUAD], [0, HALF], [R, F]]),
                    bass.AP(e.tensor, d0, [part, [1, QUAD], [R, HALF], [R, F]]), ALU.mult)
                dve.tensor_tensor(
                    z[:, QUAD * q:QUAD * (q + 1), HALF * F:NPAIR],
                    bass.AP(e.tensor, d0, [part, [1, QUAD], [R, HALF]]),
                    bass.AP(e.tensor, d0 + HALF * R, [part, [1, QUAD], [R, HALF]]),
                    ALU.mult).then_inc(z_pairs, 1)

            def z_low(t, u):
                dve.wait_ge(z_hi_ready, t * NU + u + 1)
                dve.tensor_tensor(z_lo[0:ZC, u % NC, :], ps_t[u % NC][0:ZC, :],
                                  z_hi[0:ZC, u % NC, :].bitcast(F32), ALU.subtract).then_inc(z_lo_ready, 1)

            def last_times_q(t, q):
                dve.wait_ge(last_bank_free, t * NQ + q + 2)
                if q >= 2:
                    dve.wait_ge(prod_added, t * (NQ - 1) + q - 1)
                dve.tensor_tensor(prod[:] if q else prod_sum[:], ps_q[q % 2][:], last_sb[:, q % 2, :],
                                  ALU.mult).then_inc(prod_ready, 1)

            def add_product(t, q):
                dve.wait_ge(prod_ready, t * NQ + q + 1)
                if q >= 2:
                    dve.wait_ge(prod_added, t * (NQ - 1) + q - 1)
                dve.tensor_tensor(prod_sum[:], prod_sum[:], prod[:], ALU.add).then_inc(prod_added, 1)

            def first_order_and_fm(t, b):
                dve.tensor_reduce(fsum[:], emb[b][:, 0:F, :].rearrange("p f r -> p r f"), AX.X,
                                  ALU.add).then_inc(fsum_ready, 1)
                dve.wait_ge(fsum_ready, t + 1)
                dve.tensor_tensor_reduce(fsum_sq[:], fsum[:, 0:D], fsum[:, 0:D], 1.0, 0.0, ALU.mult, ALU.add,
                                         ssq[:]).then_inc(ssq_ready, 1)
                dve.wait_ge(sq_ready, t + 1)
                dve.tensor_copy(ix_now[b][:], row_ix[:, bass.ds(t + BUF, 1), :].rearrange("p o f -> p (o f)")
                                ).then_inc(gather_ready[b], 1)
                dve.wait_ge(ssq_ready, t + 1)
                dve.tensor_tensor(fm2[:], ssq[:], sq[:], ALU.subtract).then_inc(fm2_ready, 1)
                dve.wait_ge(fm2_ready, t + 1)
                dve.scalar_tensor_tensor(lin_fm[:], fm2[:], 0.5, fsum[:, D:R], ALU.mult,
                                         ALU.add).then_inc(lin_fm_ready, 1)

            def finish_tile(t):
                dve.wait_ge(h2_done, t + 1)
                dve.scalar_tensor_tensor(h2w3[:], ps_mlp[:, 0:H], 0.0, w3_all[:], ALU.max, ALU.mult,
                                         accum_out=mlp_out[:]).then_inc(mlp_bank_free, 1)
                dve.wait_ge(mlp_bank_free, t + 2)
                dve.wait_ge(lin_fm_ready, t + 1)
                dve.scalar_tensor_tensor(partial[:], mlp_out[:], bias[:, 0:1], lin_fm[:], ALU.add,
                                         ALU.add).then_inc(partial_ready, 1)
                dve.wait_ge(partial_ready, t + 1)
                dve.wait_ge(y_done, t + 1)
                dve.tensor_tensor(y[:, bass.ds(t, 1)], ps_y[:, 0:1], partial[:], ALU.add).then_inc(tile_ready, 1)

            def between(t, after, turn, b):
                if after is not None:
                    pairs(after, b, 0)
                last_times_q(t, NQ - 1)
                if after is not None:
                    z_low(after, 0)
                add_product(t, NQ - 1)
                if after is not None:
                    z_low(after, 1)
                    pairs(after, b, 1)
                    z_low(after, 2)
                finish_tile(t)

            def tile(t, b):
                for u in range(NC, NU):
                    z_low(t, u)
                    if u == 3:
                        dve.wait_ge(embt_hi_ready, t + 1)
                        dve.tensor_tensor(embt_lo[0:EC], ps_mlp[0:EC, :].rearrange("p (c n) -> p c n", c=4),
                                          embt_hi[0:EC].bitcast(F32), ALU.subtract).then_inc(embt_lo_ready, 1)
                    if u in (3, 6):
                        pairs(t, b, u // 3 + 1)
                    if u == 7:
                        first_order_and_fm(t, b)
                    if u == 8:
                        dve.wait_ge(h1t_hi_ready, t + 1)
                        dve.tensor_tensor(h1t_lo[0:HC], ps_mlp[0:HC, :].rearrange("p (c n) -> p c n", c=4),
                                          h1t_hi[0:HC].bitcast(F32), ALU.subtract).then_inc(h1t_lo_ready, 1)
                    if u % NC == 1:
                        last_times_q(t, u // NC - 1)
                    if u % NC == 2 and u > NC * 2:
                        add_product(t, u // NC - 1)

            pairs(0, 0, 0)
            dve.wait_ge(b_copied, 2)
            dve.tensor_copy(zw[Q][:, NPAIR:NPAIR + F], b_a[:, :, F]).then_inc(zw_step[Q], 1)
            pair_weights(Q, b_a[:, :, 0:F])
            zw_low(LAST)
            z_low(0, 0)
            z_low(0, 1)
            zw_low(Q)
            z_low(0, 2)
            pairs(0, 0, 1)
            run_tiles(dve, between, tile)

        @block.tensor
        def _(pe):
            pe.wait_ge(w2_in, 16)
            pe.wait_ge(lin_in, 16 * 3)
            for g in range(F):
                mm = pe.matmul(ps_y[:, g:g + 1], w2[:, :, g], lin[:, 2:3], start=True, stop=True)
            mm.then_inc(m_done, 1)
            pe.wait_ge(w1_in, 16)
            pe.wait_ge(m_copied, 2)
            for f in range(F):
                c = (f % HALF) * (F + 1)
                mm = pe.matmul(ps_q[f // HALF][:, c:c + F + 1], w1[:, :, f], m_lin2[:], start=True, stop=True)
            mm.then_inc(b_done, 1)
            pe.wait_ge(ident_ready, 1)
            pe.wait_ge(const_ready, 3)

            def zw_transposed(o):
                pe.wait_ge(zw_step[o], zw_filled[o])
                for c in range(NC):
                    mm = pe.transpose(ps_zw[o][0:ZC, c * P:(c + 1) * P], zw[o][:, c * ZC:(c + 1) * ZC], ident[:])
                mm.then_inc(zwt_done, 1)

            def embt(t):
                pe.wait_ge(mlp_bank_free, t + 1)
                pe.wait_ge(by_pos_ready, t + 1)
                for c in range(4):
                    mm = pe.transpose(ps_mlp[0:EC, c * P:(c + 1) * P], by_pos[:, c * EC:(c + 1) * EC], ident[:])
                mm.then_inc(embt_done, 1)

            def zt(t, u):
                q, c = divmod(u, NC)
                if c == 0:
                    pe.wait_ge(z_pairs, t * NQ + q + 1)
                if u == 2:
                    pe.wait_ge(z_fields, t + 1)
                for j in range(QUAD):
                    mm = pe.transpose(ps_t[u % NC][0:ZC, j * P:(j + 1) * P],
                                      z[:, QUAD * q + j, c * ZC:(c + 1) * ZC], ident[:])
                mm.then_inc(zt_done, 1)

            def main(t, u):
                q, c = divmod(u, NC)
                pe.wait_ge(z_lo_ready, t * NU + u + 1)
                hi_x, lo_x = z_hi[0:ZC, u % NC, :], z_lo[0:ZC, u % NC, :]
                for o, ps in ((Q, ps_q[q % 2]), (LAST, ps_last)):
                    if o == LAST and c == 0:
                        pe.wait_ge(last_bank_free, t * NQ + q + 1)
                    hi_w, lo_w = zw_hi[0:ZC, o, c], zw_lo[0:ZC, o, c]
                    pe.matmul(ps[:], hi_w, lo_x, start=(c == 0), stop=False)
                    pe.matmul(ps[:], lo_w, hi_x, start=False, stop=False)
                    mm = pe.matmul(ps[:], hi_w, hi_x, start=False, stop=(c == NC - 1))
                if c == NC - 1:
                    mm.then_inc(quad_done, 1)

            def sum_products(t):
                pe.wait_ge(prod_added, (t + 1) * (NQ - 1))
                for j in range(QUAD):
                    mm = pe.matmul(ps_y[:, 0:1], prod_sum[:, j * P:(j + 1) * P], ones[:],
                                   start=(j == 0), stop=(j == QUAD - 1))
                mm.then_inc(y_done, 1)

            def hidden(x_hi, x_lo, w_hi, w_lo, k, done):
                for c in range(4):
                    kb = k + (c == 3)
                    pe.matmul(ps_mlp[:, 0:H], x_lo[0:k, c, :], w_hi[0:k, c, :], start=(c == 0), stop=False)
                    pe.matmul(ps_mlp[:, 0:H], x_hi[0:kb, c, :], w_lo[0:kb, c, :], start=False, stop=False)
                    mm = pe.matmul(ps_mlp[:, 0:H], x_hi[0:kb, c, :], w_hi[0:kb, c, :], start=False, stop=(c == 3))
                mm.then_inc(done, 1)

            def h1t(t):
                pe.wait_ge(h1_ready, t + 1)
                for c in range(4):
                    mm = pe.transpose(ps_mlp[0:HC, c * P:(c + 1) * P], h1[:, c * HC:(c + 1) * HC], ident[:])
                mm.then_inc(h1t_done, 1)

            def between(t, after, turn, b):
                if after is not None:
                    for u in range(NC):
                        zt(after, u)
                pe.wait_ge(h1t_lo_ready, t + 1)
                hidden(h1t_hi, h1t_lo, m2_hi, m2_lo, HC, h2_done)
                sum_products(t)

            def tile(t, b):
                for u in range(NU):
                    main(t, u)
                    if u + NC < NU:
                        zt(t, u + NC)
                    if u == 0:
                        embt(t)
                    if u == 2:
                        pe.wait_ge(embt_lo_ready, t + 1)
                        hidden(embt_hi, embt_lo, m1_hi, m1_lo, EC, h1_done)
                    if u == 5:
                        h1t(t)

            zw_transposed(LAST)
            for u in range(NC):
                zt(0, u)
            zw_transposed(Q)
            pe.wait_ge(m_hi_ready, 4)
            pe.wait_ge(m_lo_ready, 4)
            pe.wait_ge(zw_lo_ready, 2)
            run_tiles(pe, between, tile)


def kernel(**inputs):
    import numpy as np
    import concourse.bacc as bacc
    from concourse.bass_utils import run_bass_kernel_spmd

    nc = bacc.Bacc("TRN2", target_bir_lowering=False, num_devices=1)
    emb = np.ascontiguousarray(inputs["L0_rec_embed_table"])
    first = np.ascontiguousarray(inputs["L0_rec_w1_table"])
    fields, vocab, dim = emb.shape
    arrays = {"x_idx": np.ascontiguousarray(inputs["r_x_idx"]),
              "rows": np.concatenate([emb.reshape(fields * vocab, dim), first.reshape(fields * vocab, 1)], axis=1)}
    for name in ("w1_bias", "mlp_w1", "mlp_b1", "mlp_w2", "mlp_b2", "mlp_w3", "mlp_b3",
                 "cin_w0", "cin_w1", "cin_w2", "lin_w", "lin_b"):
        arrays[name] = np.ascontiguousarray(inputs["L0_rec_" + name])
    w1 = arrays["mlp_w1"]
    arrays["mlp_w1"] = np.ascontiguousarray(w1.reshape(fields, dim, -1).transpose(1, 0, 2)).reshape(w1.shape)
    args = [nc.dram_tensor(k, a.shape, mybir.dt.from_np(a.dtype), kind="ExternalInput").ap() for k, a in arrays.items()]
    out = nc.dram_tensor("out", (arrays["x_idx"].shape[0], 1), F32, kind="ExternalOutput").ap()
    deepfm_cin_kernel(nc, *args, out)
    return run_bass_kernel_spmd(nc, [arrays], core_ids=[0]).results[0]["out"]
```
